# Optimizing a Trainium2 kernel written in Bass

```python
import numpy as np
import jax
import jax.numpy as jnp

def _softmax(x, axis=-1):
    return jax.nn.softmax(x, axis=axis)

def _gelu(x):
    return jax.nn.gelu(x, approximate=True)

def _silu(x):
    return jax.nn.silu(x)

def _sigmoid(x):
    return jax.nn.sigmoid(x)

def _layernorm(x, axis=-1, eps=1e-05):
    m = jnp.mean(x, axis=axis, keepdims=True)
    v = jnp.var(x, axis=axis, keepdims=True)
    return (x - m) / jnp.sqrt(v + eps)

def _scatter_add(tgt, idx, src, axis=0):
    return tgt.at[idx].add(src)

def _segment_sum(src, seg, n):
    return jax.ops.segment_sum(src, seg, n)
kernel_name = 'mk_gps_d1_gnn_r8_be725e'

def setup_inputs(seed: int=0):
    np.random.seed(seed)
    _w = jnp.asarray

    def _rec_inputs():
        import jax
        import jax.numpy as jnp
        _gk = jax.random.key(seed)
        x = -0.0003713 + 1 * jax.random.normal(jax.random.fold_in(_gk, 1), (6250, 256), jnp.float32)
        _s = jax.random.randint(jax.random.fold_in(_gk, 2), (100000,), 0, 6250, jnp.int32)
        _d = jax.random.randint(jax.random.fold_in(_gk, 3), (100000,), 0, 6250, jnp.int32)
        _loop = jnp.arange(6250, dtype=jnp.int32)
        src = jnp.concatenate([_s, _d, _loop])
        dst = jnp.concatenate([_d, _s, _loop])
        _o = jnp.argsort(dst, stable=True)
        src = src[_o]
        dst = dst[_o]
        return (x, src, dst)
    x, src, dst = _rec_inputs()

    def _L0_gnn_setup():
        import jax, jax.numpy as jnp
        import numpy as np
        N, IN_CH, HEADS, OUT_CH, E = (6250, 256, 4, 64, 100000)
        key = jax.random.key(seed)
        k1, k2, k3, k4, k5 = jax.random.split(key, 5)
        x = jax.random.normal(k1, (N, IN_CH), dtype=jnp.float32)
        edge_index = jax.random.randint(k2, (2, E), 0, N, dtype=jnp.int64)
        bw = float(np.sqrt(6.0 / (IN_CH + HEADS * OUT_CH)))
        ba = float(np.sqrt(6.0 / (HEADS + OUT_CH)))
        weight = jax.random.uniform(k3, (IN_CH, HEADS * OUT_CH), jnp.float32, -bw, bw)
        attn_l = jax.random.uniform(k4, (HEADS, OUT_CH), jnp.float32, -ba, ba)
        attn_r = jax.random.uniform(k5, (HEADS, OUT_CH), jnp.float32, -ba, ba)
        return {'x': x, 'edge_index': edge_index, 'weight': weight, 'attn_l': attn_l, 'attn_r': attn_r}
    _L0_gnn_all = _L0_gnn_setup()
    _L0_gnn_in = {k: v for k, v in _L0_gnn_all.items() if k in ('weight', 'attn_l', 'attn_r')}
    del _L0_gnn_all

    def _L0_mix_setup():
        import jax, jax.numpy as jnp
        import numpy as np
        C_CURV = 1.0
        MIN_NORM = 1e-15
        BALL_EPS = 1e-05
        ATT_EPS = 1e-15
        DIM = 32

        def _norm(x):
            return jnp.clip(jnp.linalg.norm(x, axis=-1, keepdims=True), MIN_NORM)

        def proj(x, c):
            maxnorm = (1.0 - BALL_EPS) / jnp.sqrt(c)
            n = _norm(x)
            return jnp.where(n > maxnorm, x / n * maxnorm, x)

        def expmap0(u, c):
            sc = jnp.sqrt(c)
            n = _norm(u)
            return jnp.tanh(sc * n) * u / (sc * n)

        def logmap0(p, c):
            sc = jnp.sqrt(c)
            n = _norm(p)
            return jnp.arctanh(jnp.clip(sc * n, -1.0 + 1e-07, 1.0 - 1e-07)) * p / (sc * n)

        def mobius_add(x, y, c):
            x2 = jnp.sum(x * x, -1, keepdims=True)
            y2 = jnp.sum(y * y, -1, keepdims=True)
            xy = jnp.sum(x * y, -1, keepdims=True)
            num = (1 + 2 * c * xy + c * y2) * x + (1 - c * x2) * y
            den = 1 + 2 * c * xy + c * c * x2 * y2
            return num / jnp.clip(den, MIN_NORM)

        def conv1d(x, w, pad, groups=1):
            return jax.lax.conv_general_dilated(x, w, (1,), [(pad, pad)], dimension_numbers=('NCH', 'OIH', 'NCH'), feature_group_count=groups)

        def batchnorm(x, gamma, beta):
            mean = jnp.mean(x, axis=(0, 2), keepdims=True)
            var = jnp.var(x, axis=(0, 2), keepdims=True)
            xn = (x - mean) * jax.lax.rsqrt(var + 1e-05)
            return gamma[None, :, None] * xn + beta[None, :, None]

        def _reference_tuple_inner(x, w_qkv, bn_gamma, bn_beta, w_dw, w_pw, w_res, b_res):
            c = C_CURV
            h = logmap0(proj(x, c), c)
            h = jnp.transpose(h, (1, 2, 0))
            h = conv1d(h, w_qkv, pad=2)
            h = batchnorm(h, bn_gamma, bn_beta)
            h = jax.nn.relu(jnp.transpose(h, (2, 0, 1)))
            qkv = proj(expmap0(h, c), c)
            t = jnp.transpose(logmap0(proj(qkv, c), c), (1, 2, 0))
            s = conv1d(t, w_dw, pad=2, groups=t.shape[1])
            s = conv1d(s, w_pw, pad=0, groups=t.shape[1] // DIM)
            cat = jnp.concatenate([t, s], axis=1)
            ai = proj(expmap0(jnp.transpose(cat, (2, 0, 1)), c), c)
            t2 = logmap0(proj(ai, c), c)
            L, N, C2 = t2.shape
            g = C2 // (3 * DIM)
            qkv3 = jnp.transpose(t2, (1, 2, 0)).reshape(N, g, 3 * DIM, L)
            q, k, v = jnp.split(qkv3, 3, axis=2)
            q = jax.nn.relu(q)
            k = jax.nn.relu(k)
            vk = jnp.einsum('ngdl,ngel->ngde', v, k)
            out = jnp.einsum('ngde,ngdl->ngdl', vk, q)
            out = out / (jnp.sum(v, -1, keepdims=True) + ATT_EPS)
            out = jnp.transpose(out.reshape(N, g * DIM, L), (2, 0, 1))
            fx_h = proj(expmap0(out, c), c)
            ft = jnp.transpose(logmap0(proj(fx_h, c), c), (1, 2, 0))
            ft = conv1d(ft, w_res, pad=0) + b_res[None, :, None]
            fx = proj(expmap0(jnp.transpose(ft, (2, 0, 1)), c), c)
            residual = mobius_add(fx, x, c)
            return (fx, residual)
        key = jax.random.key(seed)
        ks = jax.random.split(key, 6)
        L, N, C, TD = (256, 16, 256, 256)
        x = jax.random.normal(ks[0], (L, N, C), jnp.float32) * 0.05
        w_qkv = jax.random.normal(ks[1], (3 * TD, C, 5), jnp.float32) / np.sqrt(C * 5)
        bn_gamma = jnp.ones((3 * TD,), jnp.float32)
        bn_beta = jnp.zeros((3 * TD,), jnp.float32)
        w_dw = jax.random.normal(ks[2], (3 * TD, 1, 5), jnp.float32) / np.sqrt(5.0)
        w_pw = jax.random.normal(ks[3], (3 * TD, DIM, 1), jnp.float32) / np.sqrt(DIM)
        w_res = jax.random.normal(ks[4], (C, 2 * TD, 1), jnp.float32) / np.sqrt(2 * TD)
        b_res = jnp.zeros((C,), jnp.float32)
        return {'x': x, 'w_qkv': w_qkv, 'bn_gamma': bn_gamma, 'bn_beta': bn_beta, 'w_dw': w_dw, 'w_pw': w_pw, 'w_res': w_res, 'b_res': b_res}
    _L0_mix_all = _L0_mix_setup()
    _L0_mix_in = {k: v for k, v in _L0_mix_all.items() if k in ('w_qkv', 'bn_gamma', 'bn_beta', 'w_dw', 'w_pw', 'w_res', 'b_res')}
    del _L0_mix_all

    def _L0_ffn_setup():
        import math
        import jax, jax.numpy as jnp
        import numpy as np
        CAPACITY_FACTOR = 1.25
        TOP_K = 2
        LN_EPS = 1e-05

        def _layer_norm(x, gamma, beta):
            mu = jnp.mean(x, axis=-1, keepdims=True)
            var = jnp.var(x, axis=-1, keepdims=True)
            return (x - mu) * jax.lax.rsqrt(var + LN_EPS) * gamma + beta
        key = jax.random.key(seed)
        ks = jax.random.split(key, 4)
        B, S, D, F, E = (8, 512, 256, 512, 8)
        x = jax.random.normal(ks[0], (B, S, D), dtype=jnp.float32)
        Wr = jax.random.normal(ks[1], (D, E), dtype=jnp.float32) / np.sqrt(D)
        br = jnp.zeros((E,), jnp.float32)
        W1 = jax.random.normal(ks[2], (E, D, F), dtype=jnp.float32) / np.sqrt(D)
        b1 = jnp.zeros((E, F), jnp.float32)
        W2 = jax.random.normal(ks[3], (E, F, D), dtype=jnp.float32) / np.sqrt(F)
        b2 = jnp.zeros((E, D), jnp.float32)
        gamma = jnp.ones((D,), jnp.float32)
        beta = jnp.zeros((D,), jnp.float32)
        return {'x': x, 'Wr': Wr, 'br': br, 'W1': W1, 'b1': b1, 'W2': W2, 'b2': b2, 'gamma': gamma, 'beta': beta}
    _L0_ffn_all = _L0_ffn_setup()
    _L0_ffn_in = {k: v for k, v in _L0_ffn_all.items() if k in ('Wr', 'br', 'W1', 'b1', 'W2', 'b2', 'gamma', 'beta')}
    del _L0_ffn_all
    return {'x': x, 'src': src, 'dst': dst, 'L0_gnn_weight': _L0_gnn_in['weight'], 'L0_gnn_attn_l': _L0_gnn_in['attn_l'], 'L0_gnn_attn_r': _L0_gnn_in['attn_r'], 'L0_mix_w_qkv': _L0_mix_in['w_qkv'], 'L0_mix_bn_gamma': _L0_mix_in['bn_gamma'], 'L0_mix_bn_beta': _L0_mix_in['bn_beta'], 'L0_mix_w_dw': _L0_mix_in['w_dw'], 'L0_mix_w_pw': _L0_mix_in['w_pw'], 'L0_mix_w_res': _L0_mix_in['w_res'], 'L0_mix_b_res': _L0_mix_in['b_res'], 'L0_ffn_Wr': _L0_ffn_in['Wr'], 'L0_ffn_br': _L0_ffn_in['br'], 'L0_ffn_W1': _L0_ffn_in['W1'], 'L0_ffn_b1': _L0_ffn_in['b1'], 'L0_ffn_W2': _L0_ffn_in['W2'], 'L0_ffn_b2': _L0_ffn_in['b2'], 'L0_ffn_gamma': _L0_ffn_in['gamma'], 'L0_ffn_beta': _L0_ffn_in['beta']}

def reference(x, src, dst, L0_gnn_weight, L0_gnn_attn_l, L0_gnn_attn_r, L0_mix_w_qkv, L0_mix_bn_gamma, L0_mix_bn_beta, L0_mix_w_dw, L0_mix_w_pw, L0_mix_w_res, L0_mix_b_res, L0_ffn_Wr, L0_ffn_br, L0_ffn_W1, L0_ffn_b1, L0_ffn_W2, L0_ffn_b2, L0_ffn_gamma, L0_ffn_beta):
    import jax
    import jax.numpy as jnp

    def _L0_gnn_ref(x, edge_index, weight, attn_l, attn_r):
        import jax, jax.numpy as jnp
        import numpy as np
        N, IN_CH, HEADS, OUT_CH, E = (6250, 256, 4, 64, 100000)
        heads, out_ch = attn_l.shape
        n = x.shape[0]
        xt = jnp.matmul(x, weight).reshape(-1, heads, out_ch)
        row, col = (edge_index[0], edge_index[1])
        alpha_l = jnp.einsum('ehd,hd->eh', xt[row], attn_l)
        alpha_r = jnp.einsum('ehd,hd->eh', xt[col], attn_r)
        alpha = jax.nn.softmax(jax.nn.leaky_relu(alpha_l + alpha_r, 0.01), axis=1)
        tmp = jnp.einsum('nh,nhd->nd', alpha[:n], xt[col[:n]])
        out = jnp.broadcast_to(tmp[:, None, :], (n, heads, out_ch))
        return out.reshape(n, heads * out_ch)

    def _L0_mix_ref(x, w_qkv, bn_gamma, bn_beta, w_dw, w_pw, w_res, b_res):
        import jax, jax.numpy as jnp
        import numpy as np
        C_CURV = 1.0
        MIN_NORM = 1e-15
        BALL_EPS = 1e-05
        ATT_EPS = 1e-15
        DIM = 32

        def _norm(x):
            return jnp.clip(jnp.linalg.norm(x, axis=-1, keepdims=True), MIN_NORM)

        def proj(x, c):
            maxnorm = (1.0 - BALL_EPS) / jnp.sqrt(c)
            n = _norm(x)
            return jnp.where(n > maxnorm, x / n * maxnorm, x)

        def expmap0(u, c):
            sc = jnp.sqrt(c)
            n = _norm(u)
            return jnp.tanh(sc * n) * u / (sc * n)

        def logmap0(p, c):
            sc = jnp.sqrt(c)
            n = _norm(p)
            return jnp.arctanh(jnp.clip(sc * n, -1.0 + 1e-07, 1.0 - 1e-07)) * p / (sc * n)

        def mobius_add(x, y, c):
            x2 = jnp.sum(x * x, -1, keepdims=True)
            y2 = jnp.sum(y * y, -1, keepdims=True)
            xy = jnp.sum(x * y, -1, keepdims=True)
            num = (1 + 2 * c * xy + c * y2) * x + (1 - c * x2) * y
            den = 1 + 2 * c * xy + c * c * x2 * y2
            return num / jnp.clip(den, MIN_NORM)

        def conv1d(x, w, pad, groups=1):
            return jax.lax.conv_general_dilated(x, w, (1,), [(pad, pad)], dimension_numbers=('NCH', 'OIH', 'NCH'), feature_group_count=groups)

        def batchnorm(x, gamma, beta):
            mean = jnp.mean(x, axis=(0, 2), keepdims=True)
            var = jnp.var(x, axis=(0, 2), keepdims=True)
            xn = (x - mean) * jax.lax.rsqrt(var + 1e-05)
            return gamma[None, :, None] * xn + beta[None, :, None]

        def _reference_tuple_inner(x, w_qkv, bn_gamma, bn_beta, w_dw, w_pw, w_res, b_res):
            c = C_CURV
            h = logmap0(proj(x, c), c)
            h = jnp.transpose(h, (1, 2, 0))
            h = conv1d(h, w_qkv, pad=2)
            h = batchnorm(h, bn_gamma, bn_beta)
            h = jax.nn.relu(jnp.transpose(h, (2, 0, 1)))
            qkv = proj(expmap0(h, c), c)
            t = jnp.transpose(logmap0(proj(qkv, c), c), (1, 2, 0))
            s = conv1d(t, w_dw, pad=2, groups=t.shape[1])
            s = conv1d(s, w_pw, pad=0, groups=t.shape[1] // DIM)
            cat = jnp.concatenate([t, s], axis=1)
            ai = proj(expmap0(jnp.transpose(cat, (2, 0, 1)), c), c)
            t2 = logmap0(proj(ai, c), c)
            L, N, C2 = t2.shape
            g = C2 // (3 * DIM)
            qkv3 = jnp.transpose(t2, (1, 2, 0)).reshape(N, g, 3 * DIM, L)
            q, k, v = jnp.split(qkv3, 3, axis=2)
            q = jax.nn.relu(q)
            k = jax.nn.relu(k)
            vk = jnp.einsum('ngdl,ngel->ngde', v, k)
            out = jnp.einsum('ngde,ngdl->ngdl', vk, q)
            out = out / (jnp.sum(v, -1, keepdims=True) + ATT_EPS)
            out = jnp.transpose(out.reshape(N, g * DIM, L), (2, 0, 1))
            fx_h = proj(expmap0(out, c), c)
            ft = jnp.transpose(logmap0(proj(fx_h, c), c), (1, 2, 0))
            ft = conv1d(ft, w_res, pad=0) + b_res[None, :, None]
            fx = proj(expmap0(jnp.transpose(ft, (2, 0, 1)), c), c)
            residual = mobius_add(fx, x, c)
            return (fx, residual)
        return _reference_tuple_inner(x, w_qkv, bn_gamma, bn_beta, w_dw, w_pw, w_res, b_res)[0]

    def _L0_ffn_ref(x, Wr, br, W1, b1, W2, b2, gamma, beta):
        import math
        import jax, jax.numpy as jnp
        import numpy as np
        CAPACITY_FACTOR = 1.25
        TOP_K = 2
        LN_EPS = 1e-05

        def _layer_norm(x, gamma, beta):
            mu = jnp.mean(x, axis=-1, keepdims=True)
            var = jnp.var(x, axis=-1, keepdims=True)
            return (x - mu) * jax.lax.rsqrt(var + LN_EPS) * gamma + beta
        B, S, D = x.shape
        E = Wr.shape[1]
        N = B * S
        K = TOP_K
        logits = jnp.mean(x, axis=1) @ Wr + br
        routing_weights = jax.nn.softmax(logits, axis=-1)
        capacity = float(math.ceil(N * CAPACITY_FACTOR / E))
        expected_loads = routing_weights.sum(axis=0) * (N / B)
        scale = jnp.where(expected_loads > capacity, capacity / expected_loads, 1.0)
        routing_weights = jax.nn.softmax(routing_weights * scale, axis=-1)
        rw_tok = jnp.broadcast_to(routing_weights[:, None, :], (B, S, E)).reshape(N, E)
        top_w, top_i = jax.lax.top_k(rw_tok, K)
        top_w = jax.nn.softmax(top_w, axis=-1)
        xf = x.reshape(N, D)
        h = jax.nn.gelu(jnp.einsum('nd,edf->enf', xf, W1) + b1[:, None, :], approximate=False)
        y = jnp.einsum('enf,efd->end', h, W2) + b2[:, None, :]
        w_dense = jnp.zeros((N, E), x.dtype).at[jnp.arange(N)[:, None], top_i].add(top_w)
        out = jnp.einsum('ne,end->nd', w_dense, y).reshape(B, S, D)
        out = _layer_norm(out + x, gamma, beta)
        return out
    edge_index = jnp.stack([src, dst])
    xn = _layernorm(x, axis=-1)
    x = x + _L0_gnn_ref(xn, edge_index, L0_gnn_weight, L0_gnn_attn_l, L0_gnn_attn_r) + _L0_mix_ref(xn[None], L0_mix_w_qkv, L0_mix_bn_gamma, L0_mix_bn_beta, L0_mix_w_dw, L0_mix_w_pw, L0_mix_w_res, L0_mix_b_res)[0]
    x = x + _L0_ffn_ref(_layernorm(x, axis=-1)[None], L0_ffn_Wr, L0_ffn_br, L0_ffn_W1, L0_ffn_b1, L0_ffn_W2, L0_ffn_b2, L0_ffn_gamma, L0_ffn_beta)[0]
    return x

_drawn_inputs = setup_inputs


def setup_inputs(seed=0):
    import zlib

    import numpy as np

    out = dict(_drawn_inputs(seed))
    spreads = {'L0_mix_bn_gamma': (1.0, 0.6),
     'L0_mix_bn_beta': (0.0, 0.574),
     'L0_mix_b_res': (0.0, 0.451),
     'L0_ffn_br': (0.0, 0.1),
     'L0_ffn_b1': (0.0, 0.407),
     'L0_ffn_b2': (0.0, 0.275),
     'L0_ffn_gamma': (1.0, 0.2),
     'L0_ffn_beta': (0.0, 0.1)}
    factors = {'L0_mix_w_dw': 8.0, 'L0_mix_w_pw': 8.0, 'L0_ffn_Wr': 8.0}
    for name, (base, spread) in spreads.items():
        noise = np.random.default_rng([zlib.crc32(name.encode()), seed]).standard_normal(out[name].shape)
        drawn = base * np.exp(spread * noise) if base else spread * noise
        out[name] = jnp.asarray(drawn.astype(out[name].dtype))
    for name, factor in factors.items():
        out[name] = (out[name] * factor).astype(out[name].dtype)
    return out
```

```python
import math
from contextlib import ExitStack

import concourse.bass as bass
from concourse import mybir

F32 = mybir.dt.float32
I32 = mybir.dt.int32
U32 = mybir.dt.uint32
ALU = mybir.AluOpType
ACT = mybir.ActivationFunctionType
AX = mybir.AxisListType

LN_EPS = 1e-5
BALL_EPS = 1e-5
ATT_EPS = 1e-15
MIN_NORM = 1e-15
MAXNORM = 1.0 - BALL_EPS
A_MAX = math.atanh(MAXNORM)
HEADS = 4
TOP_K = 2
CAPACITY_FACTOR = 1.25
TP = 125
TB = 2
BT = TP * TB
GROUP = 32


class Stage:

    def __init__(self, sem, per):
        self.sem, self.per = sem, per

    def count(self, b, k=None):
        return b * self.per + (self.per if k is None else k)


def older(b, n):
    return not isinstance(b, int) or b >= n


def turns(b, parity, per, more=0):
    return b // 2 * per + more if isinstance(b, int) else (b - parity) * (per // 2) + more


def wait_apart(eng, stage, value, passed):
    eng.wait_ge(stage.sem, value)
    eng.sem_inc(passed[eng.engine], 1)


def pipeline(eng, blocks, stages):
    last = max(lag for lag, _ in stages)
    head = last + 2
    pairs = (blocks - head) // 2
    for s in range(head):
        for lag, stage in stages:
            if s >= lag:
                stage(s - lag, (s - lag) % 2)
    with eng.Fori(head, head + 2 * pairs - 1, 2) as s:
        for i in range(2):
            for lag, stage in stages:
                stage(s + (i - lag), (head + i - lag) % 2)
    for s in range(head + 2 * pairs, blocks + last):
        for lag, stage in stages:
            if s - lag < blocks:
                stage(s - lag, (s - lag) % 2)


def gps_layer(nc, x, idx_dst, idx_src, w_gnn, attn_l, attn_r, w_qkv, bn_gamma, bn_beta, w_dw, w_pw,
              w_res, b_res, w_router, b_router, w1, b1, w2, b2, gamma, beta, out):
    N, D = x.shape
    KD = D // 128
    CQ = w_qkv.shape[1]
    NC = CQ // 128
    CC = 2 * CQ
    GC = CC // (3 * GROUP)
    CO = GC * GROUP
    NO = CO // 128
    XT = D + 2 * HEADS
    HD = D // HEADS
    EX, _, FF = w1.shape
    NF = FF // 128
    NB = N // BT
    NT = N // TP
    LOADS = 5
    assert NB * BT == N and NT % LOADS == 0
    CAP = math.ceil(N * CAPACITY_FACTOR / EX) / N

    xt_table = nc.dram_tensor("xt_table", (N, XT), F32, kind="Internal").ap()
    left_table = nc.dram_tensor("left_table", (N, HEADS), F32, kind="Internal").ap()

    with ExitStack() as ctx:
        def sb(name, shape, dt=F32):
            return ctx.enter_context(nc.sbuf_tensor(name, shape, dt))

        def sem(name):
            return ctx.enter_context(nc.semaphore(name))

        def stage(name, per):
            return Stage(sem(name), per)

        ps = ctx.enter_context(nc.psum_tensor("ps", [128, 8, 512], F32))

        X = sb("X", [128, NT, D])
        hT = sb("hT", [128, KD, NB, BT])
        ident = sb("ident", [128, 128])
        ones = sb("ones", [128, 128])
        phalf = sb("phalf", [128, NT])
        nhalf = sb("nhalf", [128, NT])
        wq = sb("wq", [128, KD, CQ])
        pw = sb("pw", [128, NC, 128])
        dwc = sb("dwc", [128, NC])
        wg = sb("wg", [128, KD, XT])
        wr = sb("wr", [128, NO, D])
        brow = sb("brow", [128, D])
        bng = sb("bng", [128, NC])
        bnb = sb("bnb", [128, NC])
        rt_w = sb("rt_w", [128, KD, EX])
        rt_b = sb("rt_b", [1, EX])
        gam = sb("gam", [128, D])
        bet = sb("bet", [128, D])
        idst = sb("idst", [128, NT], I32)
        isrc = sb("isrc", [128, NT], I32)
        bn_s = sb("bn_s", [128, NC])
        bn_o = sb("bn_o", [128, NC])
        mean2 = sb("mean2", [128, NT])
        rstd2 = sb("rstd2", [128, NT])
        rsum = sb("rsum", [128, KD, NB])
        rtot = sb("rtot", [128, KD])
        st = sb("st", [128, NT, 6])
        rows = sb("rows", [128, 12, NT])
        hr = sb("hr", [128, 2, NC, BT])
        cat = sb("cat", [128, 2, TB, CC])
        xts = sb("xts", [128, 2, TB, XT])
        junk = sb("junk", [128, CC])
        sums = sb("sums", [128, 3, 2, TB])
        sc = sb("sc", [128, 2, 7, TB])
        se = sb("se", [128, 2, 6, TB])
        sg = sb("sg", [128, 2, 6, TB])
        veps = sb("veps", [128, TB, GC, GROUP])
        krel = sb("krel", [128, TB, GC // 2, GROUP])
        rv = sb("rv", [128, GC, GROUP])
        qk = sb("qk", [128, GC, GROUP])
        vr = sb("vr", [128, GC, GROUP])
        ksum = sb("ksum", [128, GC])
        ob = sb("ob", [128, 2, TB, CO])
        oT = sb("oT", [128, TB, NO, TP])
        u = sb("u", [128, 2, TB, D])
        ist = sb("ist", [128, 2, 2 * TB], I32)
        xg = sb("xg", [128, 2, TB, XT])
        asrc = sb("asrc", [128, 2, TB, HEADS])
        at = sb("at", [128, 6, TB, HEADS])
        atm = sb("atm", [128, 3, TB])
        gprod = sb("gprod", [128, D])
        gt = sb("gt", [128, 2, TB, HD])
        st2 = sb("st2", [128, TB, 6])
        mv2 = sb("mv2", [128, 2, TB, 2])
        r2 = sb("r2", [128, 2, 2, TB])
        xn = xts[:, :, :, 0:D]
        flat_hr = hr[:, :, :, :].rearrange("p a c n -> p (a c n)")
        hb = flat_hr[:, 0:2 * TB * (D + 1)].rearrange("p (a t d) -> p a t d", a=2, t=TB)
        hTs = flat_hr[:, 1040:1040 + 2 * KD * BT].rearrange("p (a k n) -> p a k n", a=2, k=KD)
        w1s = flat_hr[:, 0:TOP_K * KD * FF].rearrange("p (i k f) -> p i k f", i=TOP_K, k=KD)
        b2s = flat_hr[:, TOP_K * KD * FF:TOP_K * KD * FF + TOP_K * D].rearrange("p (i d) -> p i d", i=TOP_K)
        flat = cat[:, :, :, :].rearrange("p a t c -> p (a t c)")
        spill = junk[:].bitcast(mybir.dt.bfloat16)
        spill_cat, spill_att, spill_u = spill[0:TP, 0:CC], spill[0:TP, CC:CC + CO], spill[0:TP, CC + CO:CC + CO + D]
        gram = flat[:, 0:2 * (D + 1)].rearrange("p (k d) -> p k d", k=KD)
        wgw = flat[:, 1024:1024 + KD * CQ].rearrange("p (k c) -> p k c", k=KD)
        attb = flat[:, 2560:2560 + 2 * D].rearrange("p (s d) -> p s d", s=2)
        attp = flat[:, 3072:3072 + 2 * KD * D].rearrange("p (s k d) -> p s k d", s=2, k=KD)
        bst = sb("bst", [128, 8, NC])
        ge = flat[:, 0:2 * 2 * NF * BT].rearrange("p (a f n) -> p a f n", a=2, f=TOP_K * NF)
        w2s = flat[:, 4032:4032 + TOP_K * NF * D].rearrange("p (i f d) -> p i f d", i=TOP_K, f=NF)
        b1s = sb("b1s", [128, TOP_K, NF])
        b2w = sb("b2w", [128, D])
        rt = sb("rt", [1, 24, EX])
        iota = sb("iota", [1, EX])
        chosen = sb("chosen", [1, TOP_K], I32)
        tw = sb("tw", [128, TOP_K])
        za = ob[:, :, :, 0:D]
        zz = u
        zst = sb("zst", [128, TB, 6])
        zmv = sb("zmv", [128, 2, TB, 2])
        zr = sb("zr", [128, 2, 2, TB])
        yo = xts[:, :, :, 0:D]

        x_in = [sem(f"x_in{i}") for i in range(LOADS)]
        w_in = sem("w_in")
        late_in = sem("late_in")
        xt_out = [sem("xt_out0"), sem("xt_out1")]
        gathered = [sem("gathered0"), sem("gathered1")]
        experts_in = sem("experts_in")
        y_out = [sem("y_out0"), sem("y_out1")]
        const = sem("const")
        prep = sem("prep")
        sums_done = sem("sums_done")
        row_dve = sem("row_dve")
        row_pool = sem("row_pool")
        row_ln = sem("row_ln")
        h_made = stage("h_made", TB)
        h_turned = stage("h_turned", 1)
        h_out = stage("h_out", 1)
        gram_done = stage("gram_done", 1)
        xt_made = stage("xt_made", TB)
        xt_ready = stage("xt_ready", TB)
        h_kept = stage("h_kept", 1)
        bn_pe = sem("bn_pe")
        bn_dve = sem("bn_dve")
        bn_pool = sem("bn_pool")
        qkv_done = stage("qkv_done", NC)
        relu_done = stage("relu_done", NC)
        cat_done = stage("cat_done", TB)
        cat_out = stage("cat_out", TB)
        cat_sq = stage("cat_sq", TB)
        scale_c = stage("scale_c", 7)
        kv_ready = stage("kv_ready", 2 * TB)
        att = stage("att", 6 * TB)
        att_sq = stage("att_sq", TB)
        scale_e = stage("scale_e", 6)
        o_turned = stage("o_turned", TB)
        o_out = stage("o_out", TB)
        res_done = stage("res_done", 1)
        u_made = stage("u_made", TB)
        u_sq = stage("u_sq", TB)
        scale_g = stage("scale_g", 5)
        tanh_done = stage("tanh_done", 1)
        idx_ready = stage("idx_ready", 2)
        edge = stage("edge", 7 + 2 * TB)
        edge_exp = stage("edge_exp", 1)
        x1 = stage("x1", 4 * TB)
        rstd_done = stage("rstd_done", 2)
        xn_made = stage("xn_made", TB + 2)
        xn_turned = stage("xn_turned", 1)
        xn_kept = stage("xn_kept", 2)
        rt_pe = sem("rt_pe")
        rt_dve = sem("rt_dve")
        rt_act = sem("rt_act")
        tw_pe = sem("tw_pe")
        w_dve = sem("w_dve")
        f_done = stage("f_done", TOP_K * NF)
        gelu_done = stage("gelu_done", TOP_K * NF)
        y_done = stage("y_done", TB)
        z = stage("z", 5 * TB)
        z_rstd = stage("z_rstd", 2)
        z_norm = stage("z_norm", TB)
        z_gam = stage("z_gam", 2 * TB)
        y_ready = stage("y_ready", TB)

        passed = {e.engine: sem(f"passed{i}") for i, e in enumerate((nc.vector, nc.gpsimd))}

        block = ctx.enter_context(nc.Block())

        tok = lambda a: a.rearrange("(b p t) d -> p b t d", p=TP, t=TB)
        xv, ov = tok(x), tok(out)
        xt_rows, left_rows = tok(xt_table), tok(left_table)
        X4 = X[0:TP, :, :].rearrange("p (b t) d -> p b t d", t=TB)
        W_IN = 11
        LATE = 5

        ROW_DVE1, ROW_DVE2, ROW_DVE3, ROW_DVE4 = 8, 10, 15, 19
        PREP = 3 + 2 * KD
        BN_READ, BN_VAR, BN_DONE = 9, 12, 15
        RT_E1 = 4
        RT_E2 = 10
        RT_CHOSEN = 14 + 6 * TOP_K + 1
        RT_E3 = RT_CHOSEN + 1
        RT_TW = RT_E3 + 3
        half = NC // 2

        @block.sync
        def _(sp):
            per = NB // LOADS
            for i in range(LOADS):
                sp.dma_start(X4[:, i * per:(i + 1) * per].rearrange("p b t d -> p b (t d)"),
                             xv[:, i * per:(i + 1) * per].rearrange("p b t d -> p b (t d)")).then_inc(x_in[i], 16)

            def store(b, par):
                sp.wait_ge(xt_ready.sem, xt_ready.count(b))
                sp.dma_start(xt_rows[:, b], xts[0:TP, par, :, :]).then_inc(xt_out[par], 16)
                sp.dma_start(left_rows[:, b], xts[0:TP, par, :, D:D + HEADS]).then_inc(xt_out[par], 16)

            pipeline(sp, NB, [(0, store)])

            sp.wait_ge(rt_dve, RT_CHOSEN)
            for i in range(TOP_K):
                e = sp.value_load(chosen[0:1, i:i + 1], min_val=0, max_val=EX - 1)
                sp.dma_start(w1s[:, i, :, :], w1[e].rearrange("(k p) f -> p k f", p=128)).then_inc(experts_in, 16)
                sp.dma_start(w2s[:, i, :, :], w2[e].rearrange("(k p) f -> p k f", p=128)).then_inc(experts_in, 16)
                sp.dma_start(b1s[:, i, :], b1[e].rearrange("(k p) -> p k", p=128),
                             allow_slow_non_contiguous=True).then_inc(experts_in, 16)
                sp.dma_start(b2s[0:TP, i, :], b2[bass.ds(e, 1)].broadcast_to([TP, D])).then_inc(experts_in, 16)

            def give(b, par):
                sp.wait_ge(y_ready.sem, y_ready.count(b))
                sp.dma_start(ov[:, b], yo[0:TP, par, :, :]).then_inc(y_out[par], 16)

            pipeline(sp, NB, [(0, give)])
            sp.wait_ge(y_out[0], 16 * ((NB + 1) // 2))
            sp.wait_ge(y_out[1], 16 * (NB // 2))
            sp.wait_ge(xt_out[0], 32 * ((NB + 1) // 2))
            sp.wait_ge(xt_out[1], 32 * (NB // 2))

        @block.gpsimd
        def _(pool):
            nc.gpsimd.memset(ident[:], 0.0).then_inc(const, 1)
            nc.gpsimd.memset(ones[:], 1.0).then_inc(const, 1)
            nc.gpsimd.memset(phalf[:], 0.5).then_inc(const, 1)
            nc.gpsimd.memset(nhalf[:], -0.5).then_inc(const, 1)
            nc.gpsimd.memset(hb[:, :, :, D:D + 1], 1.0).then_inc(const, 1)
            nc.gpsimd.iota(iota[:], [[1, EX]], base=0, channel_multiplier=0,
                           allow_small_or_imprecise_dtypes=True).then_inc(const, 1)
            pool.wait_ge(const, 6)
            nc.gpsimd.affine_select(out=ident[:], in_=ident[:], compare_op=ALU.not_equal, fill=1.0, base=0,
                                    pattern=[[-1, 128]], channel_multiplier=1).then_inc(const, 1)
            pool.wait_ge(row_dve, ROW_DVE1)
            nc.gpsimd.tensor_tensor(rows[0:TP, 5, :], rows[0:TP, 4, :], nhalf[0:TP, :], ALU.pow).then_inc(row_pool, 1)
            pool.wait_ge(row_dve, ROW_DVE2)
            nc.gpsimd.tensor_tensor(rows[0:TP, 7, :], rows[0:TP, 6, :], phalf[0:TP, :], ALU.pow).then_inc(row_pool, 1)
            pool.wait_ge(bn_dve, BN_VAR)
            nc.gpsimd.tensor_tensor(bst[:, 5, :], bst[:, 4, :], nhalf[:, 0:NC], ALU.pow).then_inc(bn_pool, 1)

            def scale_of_cat(b, par):
                if older(b, 2):
                    pool.wait_ge(scale_e.sem, scale_e.count(b - 2))
                    pool.wait_ge(kv_ready.sem, kv_ready.count(b - 2))
                wait_apart(pool, cat_sq, cat_sq.count(b), passed)
                s, n = sc[0:TP, par], scale_c
                nc.gpsimd.tensor_scalar(s[:, 0], sums[0:TP, 0, par], MIN_NORM ** 2, None, ALU.max).then_inc(n.sem, 1)
                pool.wait_ge(n.sem, n.count(b, 1))
                nc.gpsimd.tensor_tensor(s[:, 1], s[:, 0], nhalf[0:TP, 0:TB], ALU.pow).then_inc(n.sem, 1)
                wait_apart(pool, n, n.count(b, 2), passed)
                nc.gpsimd.tensor_scalar(s[:, 2], s[:, 1], A_MAX, 1.0, ALU.mult, ALU.min).then_inc(n.sem, 1)
                nc.gpsimd.tensor_tensor(s[:, 4], s[:, 0], s[:, 1], ALU.mult).then_inc(n.sem, 1)
                pool.wait_ge(n.sem, n.count(b, 4))
                nc.gpsimd.tensor_tensor(s[:, 3], s[:, 2], s[:, 2], ALU.mult).then_inc(n.sem, 1)
                nc.gpsimd.tensor_scalar(s[:, 5], s[:, 4], 1.0 / A_MAX, 1.0, ALU.mult, ALU.max).then_inc(n.sem, 1)
                wait_apart(pool, n, n.count(b, 6), passed)
                nc.gpsimd.tensor_scalar(s[:, 6], s[:, 5], ATT_EPS, None, ALU.mult).then_inc(n.sem, 1)

            def kv(b, par):
                pool.wait_ge(scale_c.sem, scale_c.count(b))
                wait_apart(pool, cat_out, cat_out.count(b), passed)
                for t in range(TB):
                    if older(b, 1):
                        wait_apart(pool, att, att.count(b - 1, 6 * (t + 1)), passed)
                    c = cat[0:TP, par, t].rearrange("p (g c) -> p g c", c=3 * GROUP)
                    nc.gpsimd.tensor_scalar(veps[0:TP, t], c[:, :, 2 * GROUP:], sc[0:TP, par, 6, t:t + 1], None,
                                            ALU.add).then_inc(kv_ready.sem, 1)
                    nc.gpsimd.tensor_scalar(krel[0:TP, t], c[:, GC // 2:, GROUP:2 * GROUP], 0.0, None,
                                            ALU.max).then_inc(kv_ready.sem, 1)

            def scale_of_att(b, par):
                if older(b, 2):
                    pool.wait_ge(u_made.sem, u_made.count(b - 2))
                wait_apart(pool, att_sq, att_sq.count(b), passed)
                s, n = se[0:TP, par], scale_e
                nc.gpsimd.tensor_scalar(s[:, 0], sums[0:TP, 1, par], MIN_NORM ** 2, None, ALU.max).then_inc(n.sem, 1)
                pool.wait_ge(n.sem, n.count(b, 1))
                nc.gpsimd.tensor_tensor(s[:, 1], s[:, 0], nhalf[0:TP, 0:TB], ALU.pow).then_inc(n.sem, 1)
                pool.wait_ge(n.sem, n.count(b, 2))
                nc.gpsimd.tensor_tensor(s[:, 2], s[:, 1], sc[0:TP, par, 5], ALU.mult).then_inc(n.sem, 1)
                pool.wait_ge(n.sem, n.count(b, 3))
                nc.gpsimd.tensor_tensor(s[:, 3], s[:, 2], sc[0:TP, par, 5], ALU.mult).then_inc(n.sem, 1)
                wait_apart(pool, n, n.count(b, 4), passed)
                nc.gpsimd.tensor_scalar(s[:, 4], s[:, 3], A_MAX, 1.0, ALU.mult, ALU.min).then_inc(n.sem, 1)
                pool.wait_ge(n.sem, n.count(b, 5))
                nc.gpsimd.tensor_tensor(s[:, 5], s[:, 4], sc[0:TP, par, 3], ALU.mult).then_inc(n.sem, 1)

            def scale_of_u(b, par):
                if older(b, 2):
                    pool.wait_ge(x1.sem, x1.count(b - 2))
                wait_apart(pool, u_sq, u_sq.count(b), passed)
                s, n = sg[0:TP, par], scale_g
                nc.gpsimd.tensor_scalar(s[:, 0], sums[0:TP, 2, par], MIN_NORM ** 2, None, ALU.max).then_inc(n.sem, 1)
                pool.wait_ge(n.sem, n.count(b, 1))
                nc.gpsimd.tensor_tensor(s[:, 1], s[:, 0], nhalf[0:TP, 0:TB], ALU.pow).then_inc(n.sem, 1)
                pool.wait_ge(n.sem, n.count(b, 2))
                nc.gpsimd.tensor_tensor(s[:, 2], s[:, 0], s[:, 1], ALU.mult).then_inc(n.sem, 1)
                wait_apart(pool, tanh_done, tanh_done.count(b), passed)
                nc.gpsimd.tensor_scalar(s[:, 4], s[:, 3], MAXNORM, None, ALU.min).then_inc(n.sem, 1)
                pool.wait_ge(n.sem, n.count(b, 4))
                nc.gpsimd.tensor_tensor(s[:, 5], s[:, 4], s[:, 1], ALU.mult).then_inc(n.sem, 1)

            def rstd_of_x1(b, par):
                if older(b, 2):
                    pool.wait_ge(xn_made.sem, xn_made.count(b - 2))
                wait_apart(pool, x1, x1.count(b), passed)
                nc.gpsimd.tensor_scalar(r2[0:TP, par, 0], mv2[0:TP, par, :, 1], LN_EPS, None,
                                        ALU.add).then_inc(rstd_done.sem, 1)
                pool.wait_ge(rstd_done.sem, rstd_done.count(b, 1))
                nc.gpsimd.tensor_tensor(r2[0:TP, par, 1], r2[0:TP, par, 0], nhalf[0:TP, 0:TB],
                                        ALU.pow).then_inc(rstd_done.sem, 1)

            def gather(b, par):
                if older(b, 2):
                    pool.wait_ge(edge.sem, edge.count(b - 2))
                    pool.wait_ge(gathered[par], turns(b, par, 32 * TB))
                nc.gpsimd.tensor_copy(ist[0:TP, par, 0:TB], idst[0:TP, bass.ds(b * TB, TB)]).then_inc(idx_ready.sem, 1)
                nc.gpsimd.tensor_copy(ist[0:TP, par, TB:2 * TB], isrc[0:TP, bass.ds(b * TB, TB)]).then_inc(idx_ready.sem, 1)
                wait_apart(pool, idx_ready, idx_ready.count(b), passed)
                for t in range(TB):
                    nc.gpsimd.indirect_dma_start(
                        xg[0:TP, par, t, :], None, xt_table,
                        bass.IndirectOffsetOnAxis(ap=ist[0:TP, par, t:t + 1].bitcast(U32), axis=0)).then_inc(gathered[par], 16)
                    nc.gpsimd.indirect_dma_start(
                        asrc[0:TP, par, t, :], None, left_table,
                        bass.IndirectOffsetOnAxis(ap=ist[0:TP, par, TB + t:TB + t + 1].bitcast(U32),
                                                  axis=0)).then_inc(gathered[par], 16)

            pool.wait_ge(late_in, 16 * LATE)
            pool.wait_ge(xt_out[0], 32 * ((NB + 1) // 2))
            pool.wait_ge(xt_out[1], 32 * (NB // 2))
            pipeline(pool, NB, [(2, gather), (2, kv), (3, scale_of_u), (2, scale_of_att), (1, scale_of_cat),
                                (4, rstd_of_x1)])

            def z_scale(b, par):
                if older(b, 2):
                    pool.wait_ge(z_norm.sem, z_norm.count(b - 2))
                wait_apart(pool, z, z.count(b), passed)
                nc.gpsimd.tensor_scalar(zr[0:TP, par, 0], zmv[0:TP, par, :, 1], LN_EPS, None,
                                        ALU.add).then_inc(z_rstd.sem, 1)
                pool.wait_ge(z_rstd.sem, z_rstd.count(b, 1))
                nc.gpsimd.tensor_tensor(zr[0:TP, par, 1], zr[0:TP, par, 0], nhalf[0:TP, 0:TB],
                                        ALU.pow).then_inc(z_rstd.sem, 1)

            def z_affine(b, par):
                for t in range(TB):
                    pool.wait_ge(z_norm.sem, z_norm.count(b, t + 1))
                    nc.gpsimd.tensor_tensor(zz[0:TP, par, t], zz[0:TP, par, t], gam[0:TP, :],
                                            ALU.mult).then_inc(z_gam.sem, 1)
                    pool.wait_ge(z_gam.sem, z_gam.count(b, 2 * t + 1))
                    nc.gpsimd.tensor_tensor(zz[0:TP, par, t], zz[0:TP, par, t], bet[0:TP, :],
                                            ALU.add).then_inc(z_gam.sem, 1)

            pipeline(pool, NB, [(1, z_scale), (2, z_affine)])

        @block.scalar
        def _(act):
            act.dma_start(wg[:, :, 0:D], w_gnn.rearrange("(k p) d -> p k d", p=128)).then_inc(w_in, 16)
            act.dma_start(attb[:, 0, :], attn_l.rearrange("(a h) d -> a (h d)", a=1).broadcast_to([128, D])).then_inc(w_in, 16)
            act.dma_start(attb[:, 1, :], attn_r.rearrange("(a h) d -> a (h d)", a=1).broadcast_to([128, D])).then_inc(w_in, 16)
            act.dma_start(wq[:, :, :], w_qkv.rearrange("(k p) c -> p k c", p=128)).then_inc(w_in, 16)
            act.dma_start(dwc[:, :], w_dw).then_inc(w_in, 16)
            act.dma_start(bng[:, :], bn_gamma).then_inc(w_in, 16)
            act.dma_start(bnb[:, :], bn_beta).then_inc(w_in, 16)
            act.wait_ge(prep, 1)
            for r in range(128 // GROUP):
                act.dma_start(pw[GROUP * r:GROUP * (r + 1), :, GROUP * r:GROUP * (r + 1)],
                              w_pw.rearrange("(c r) i o -> r i c o", r=128 // GROUP)[r]).then_inc(w_in, 16)
            act.dma_start(idst[0:TP, :], idx_dst).then_inc(late_in, 16)
            act.dma_start(isrc[0:TP, :], idx_src).then_inc(late_in, 16)
            act.dma_start(wr[:, :, :], w_res.rearrange("(k p) d -> p k d", p=128)).then_inc(late_in, 16)
            act.dma_start(brow[:, :], b_res.rearrange("(a d) -> a d", a=1).broadcast_to([128, D])).then_inc(late_in, 16)
            act.dma_start(rt_w[:, :, :], w_router.rearrange("(k p) e -> p k e", p=128)).then_inc(late_in, 16)
            act.dma_start(rt_b[:, :], b_router.rearrange("(a e) -> a e", a=1)).then_inc(experts_in, 16)
            act.dma_start(gam[:, :], gamma.rearrange("(a d) -> a d", a=1).broadcast_to([128, D])).then_inc(experts_in, 16)
            act.dma_start(bet[:, :], beta.rearrange("(a d) -> a d", a=1).broadcast_to([128, D])).then_inc(experts_in, 16)

            act.wait_ge(row_dve, ROW_DVE3)
            nc.scalar.activation(rows[0:TP, 8, :], rows[0:TP, 6, :], ACT.Ln).then_inc(row_ln, 1)

            def h_to_sbuf(b, par):
                act.wait_ge(h_turned.sem, h_turned.count(b))
                if older(b, 2):
                    act.wait_ge(xt_made.sem, xt_made.count(b - 2))
                    act.wait_ge(h_kept.sem, h_kept.count(b - 2))
                nc.scalar.activation(hTs[:, par].rearrange("p k n -> p (k n)"), ps[:, par, 0:KD * BT],
                                     ACT.Copy).then_inc(h_out.sem, 1)

            pipeline(act, NB, [(0, h_to_sbuf)])

            def relu(b, par, chunks):
                for c in chunks:
                    act.wait_ge(qkv_done.sem, qkv_done.count(b, c + 1))
                    if c == 0 and older(b, 2):
                        act.wait_ge(cat_done.sem, cat_done.count(b - 2))
                    nc.scalar.activation(hr[:, par, c, :], ps[:, c % 2, 0:BT], ACT.Relu, bias=bn_o[:, c:c + 1],
                                         scale=bn_s[:, c:c + 1]).then_inc(relu_done.sem, 1)

            def square_cat(b, par, t):
                act.wait_ge(cat_out.sem, cat_out.count(b, t + 1))
                if t == 0 and older(b, 2):
                    act.wait_ge(scale_c.sem, scale_c.count(b - 2, 1))
                if t == 1 or older(b, 1):
                    act.wait_ge(cat_sq.sem, b * TB + t)
                nc.scalar.activation(spill_cat, cat[0:TP, par, t, :], ACT.Square,
                                     accum_out=sums[0:TP, 0, par, t:t + 1]).then_inc(cat_sq.sem, 1)

            def square_att(b, par, t):
                act.wait_ge(att.sem, att.count(b, 6 * (t + 1)))
                if t == 0 and older(b, 2):
                    act.wait_ge(scale_e.sem, scale_e.count(b - 2, 1))
                if t == 1 or older(b, 1):
                    act.wait_ge(att_sq.sem, b * TB + t)
                nc.scalar.activation(spill_att, ob[0:TP, par, t, :], ACT.Square,
                                     accum_out=sums[0:TP, 1, par, t:t + 1]).then_inc(att_sq.sem, 1)

            def turn_out(b, par, t):
                act.wait_ge(o_turned.sem, o_turned.count(b, t + 1))
                if older(b, 1):
                    act.wait_ge(res_done.sem, res_done.count(b - 1))
                nc.scalar.activation(oT[:, t].rearrange("p c n -> p (c n)"), ps[:, 5, 0:NO * TP],
                                     ACT.Copy).then_inc(o_out.sem, 1)

            def square_u(b, par):
                for t in range(TB):
                    act.wait_ge(u_made.sem, u_made.count(b, t + 1))
                    if t == 0 and older(b, 2):
                        act.wait_ge(scale_g.sem, scale_g.count(b - 2, 1))
                    if t == 1 or older(b, 1):
                        act.wait_ge(u_sq.sem, b * TB + t)
                    nc.scalar.activation(spill_u, u[0:TP, par, t, :], ACT.Square,
                                         accum_out=sums[0:TP, 2, par, t:t + 1]).then_inc(u_sq.sem, 1)

            def tanh(b, par):
                act.wait_ge(scale_g.sem, scale_g.count(b, 3))
                nc.scalar.activation(sg[0:TP, par, 3], sg[0:TP, par, 2], ACT.Tanh).then_inc(tanh_done.sem, 1)

            def edge_softmax(b, par):
                act.wait_ge(edge.sem, edge.count(b, 4))
                nc.scalar.activation(at[0:TP, 4], at[0:TP, 3], ACT.Exp).then_inc(edge_exp.sem, 1)

            act.wait_ge(bn_dve, BN_DONE)
            pipeline(act, NB, [
                (0, lambda b, p: relu(b, p, range(half))),
                (3, lambda b, p: turn_out(b, p, 0)),
                (3, lambda b, p: turn_out(b, p, 1)),
                (3, edge_softmax),
                (0, lambda b, p: relu(b, p, range(half, NC))),
                (1, lambda b, p: square_cat(b, p, 0)),
                (2, lambda b, p: square_att(b, p, 0)),
                (3, square_u),
                (3, tanh),
                (1, lambda b, p: square_cat(b, p, 1)),
                (2, lambda b, p: square_att(b, p, 1)),
            ])

            for n, (waited, dst, src, w) in enumerate(((RT_E1, 2, 1, EX), (RT_E2, 6, 5, EX), (RT_E3, 19, 18, 1))):
                act.wait_ge(rt_dve, waited)
                nc.scalar.activation(rt[0:1, dst, 0:w], rt[0:1, src, 0:w], ACT.Exp).then_inc(rt_act, 1)

            act.wait_ge(experts_in, 16 * (3 + 4 * TOP_K))

            def gelu(b, par):
                for f in range(TOP_K * NF):
                    act.wait_ge(f_done.sem, f_done.count(b, f + 1))
                    if f == 0 and older(b, 2):
                        act.wait_ge(y_done.sem, y_done.count(b - 2))
                    nc.scalar.activation(ge[:, par, f, :], ps[:, f % 4, 0:BT], ACT.Gelu,
                                         bias=b1s[:, f // NF, f % NF:f % NF + 1]).then_inc(gelu_done.sem, 1)

            pipeline(act, NB, [(0, gelu)])

        @block.tensor
        def _(pe):
            pe.wait_ge(const, 7)
            pe.wait_ge(prep, PREP)
            nc.tensor.matmul(ps[:, 2, 0:D + 1], junk[:, 0:128], junk[:, 0:D + 1], start=True, stop=True,
                             skip_group_check=True)
            nc.tensor.matmul(ps[:, 3, 0:D + 1 - 128], junk[:, 0:128], junk[:, 0:D + 1 - 128], start=True, stop=True,
                             skip_group_check=True)

            def turn_h(b, par):
                pe.wait_ge(h_made.sem, h_made.count(b))
                if older(b, 2):
                    pe.wait_ge(h_out.sem, h_out.count(b - 2))
                for t in range(TB):
                    for k in range(KD):
                        last = nc.tensor.transpose(ps[:, par, k * BT + t * TP:k * BT + (t + 1) * TP],
                                                   hb[0:TP, par, t, k * 128:(k + 1) * 128], ident[0:TP, 0:TP])
                last.then_inc(h_turned.sem, 1)

            def add_gram(b, par):
                for t in range(TB):
                    nc.tensor.matmul(ps[:, 2, 0:D + 1], hb[0:TP, par, t, 0:128], hb[0:TP, par, t, :],
                                     start=False, stop=False, skip_group_check=True)
                    last = nc.tensor.matmul(ps[:, 3, 0:D + 1 - 128], hb[0:TP, par, t, 128:256],
                                            hb[0:TP, par, t, 128:D + 1], start=False, stop=False,
                                            skip_group_check=True)
                last.then_inc(gram_done.sem, 1)

            def make_xt(b, par):
                pe.wait_ge(h_out.sem, h_out.count(b))
                for t in range(TB):
                    if older(b, 1):
                        pe.wait_ge(xt_ready.sem, xt_ready.count(b - 1, t + 1))
                    for k in range(KD):
                        last = nc.tensor.matmul(ps[0:TP, 4 + t, 0:XT], hTs[:, par, k, t * TP:(t + 1) * TP],
                                                wg[:, k, :], start=(k == 0), stop=(k == KD - 1))
                    last.then_inc(xt_made.sem, 1)

            pipeline(pe, NB, [(0, turn_h), (0, add_gram), (1, make_xt)])

            pe.wait_ge(bn_dve, 2)
            nc.tensor.transpose(ps[:, 6, 0:128], gram[:, 0, 128:256], ident[:]).then_inc(bn_pe, 1)
            pe.wait_ge(bn_dve, 3)
            for m in range(KD):
                for n in range(2):
                    for k in range(KD):
                        last = nc.tensor.matmul(ps[:, 2 * m + n, 0:CQ // 2], gram[:, k, m * 128:(m + 1) * 128],
                                                wq[:, k, n * (CQ // 2):(n + 1) * (CQ // 2)],
                                                start=(k == 0), stop=(k == KD - 1))
            last.then_inc(bn_pe, 1)
            pe.wait_ge(bn_dve, 7)
            for c in range(NC):
                for k in range(KD):
                    nc.tensor.matmul(ps[:, 7, c:c + 1], wgw[:, k, c * 128:(c + 1) * 128], ones[:, 0:1],
                                     start=(k == 0), stop=(k == KD - 1))
                for k in range(KD):
                    last = nc.tensor.matmul(ps[:, 7, NC + c:NC + c + 1], wq[:, k, c * 128:(c + 1) * 128],
                                            gram[:, k, D:D + 1], start=(k == 0), stop=(k == KD - 1))
            last.then_inc(bn_pe, 1)

            def qkv(b, par, chunks):
                for c in chunks:
                    if c >= 2 or older(b, 1):
                        pe.wait_ge(relu_done.sem, b * NC + c - 1)
                    for k in range(KD):
                        last = nc.tensor.matmul(ps[:, c % 2, 0:BT], wq[:, k, c * 128:(c + 1) * 128], hT[:, k, b, :],
                                                start=(k == 0), stop=(k == KD - 1))
                    last.then_inc(qkv_done.sem, 1)

            catp = ps[:, 2:5, :].rearrange("p a n -> p (a n)")

            def make_cat(b, par, t):
                pe.wait_ge(relu_done.sem, relu_done.count(b))
                if t == 1 or older(b, 1):
                    pe.wait_ge(cat_out.sem, b * TB + t)
                for c in range(NC):
                    h = hr[:, par, c, t * TP:(t + 1) * TP]
                    nc.tensor.transpose(catp[0:TP, c * 128:(c + 1) * 128], h, ident[:])
                    last = nc.tensor.matmul(catp[0:TP, CQ + c * 128:CQ + (c + 1) * 128], h, pw[:, c, :],
                                            start=True, stop=True)
                last.then_inc(cat_done.sem, 1)

            def turn_att(b, par, t):
                pe.wait_ge(att.sem, att.count(b, 6 * (t + 1)))
                if t == 1 or older(b, 1):
                    pe.wait_ge(o_out.sem, b * TB + t)
                for c in range(NO):
                    last = nc.tensor.transpose(ps[:, 5, c * TP:(c + 1) * TP], ob[0:TP, par, t, c * 128:(c + 1) * 128],
                                               ident[0:TP, 0:TP])
                last.then_inc(o_turned.sem, 1)

            def res(b, par):
                pe.wait_ge(o_out.sem, o_out.count(b))
                if older(b, 1):
                    pe.wait_ge(u_made.sem, u_made.count(b - 1))
                for t in range(TB):
                    for c in range(NO):
                        last = nc.tensor.matmul(ps[0:TP, 6, t * D:(t + 1) * D], oT[:, t, c, :], wr[:, c, :],
                                                start=(c == 0), stop=(c == NO - 1))
                last.then_inc(res_done.sem, 1)

            def turn_xn(b, par):
                pe.wait_ge(xn_made.sem, xn_made.count(b, TB))
                if older(b, 1):
                    pe.wait_ge(xn_kept.sem, xn_kept.count(b - 1, 1))
                for t in range(TB):
                    for k in range(KD):
                        last = nc.tensor.transpose(ps[:, 7, k * BT + t * TP:k * BT + (t + 1) * TP],
                                                   xn[0:TP, par, t, k * 128:(k + 1) * 128], ident[0:TP, 0:TP])
                last.then_inc(xn_turned.sem, 1)

            pe.wait_ge(bn_dve, BN_READ)
            pe.wait_ge(h_kept.sem, h_kept.count(NB - 1))
            pe.wait_ge(late_in, 16 * LATE)
            pipeline(pe, NB, [
                (0, lambda b, p: qkv(b, p, range(half))),
                (3, lambda b, p: turn_att(b, p, 0)),
                (1, lambda b, p: make_cat(b, p, 0)),
                (3, lambda b, p: turn_att(b, p, 1)),
                (0, lambda b, p: qkv(b, p, range(half, NC))),
                (3, res),
                (1, lambda b, p: make_cat(b, p, 1)),
                (5, turn_xn),
            ])

            pe.wait_ge(rt_dve, 1)
            for k in range(KD):
                last = nc.tensor.matmul(ps[0:1, 0, 0:EX], rtot[:, k:k + 1], rt_w[:, k, :],
                                        start=(k == 0), stop=(k == KD - 1))
            last.then_inc(rt_pe, 1)
            pe.wait_ge(rt_dve, RT_TW)
            nc.tensor.matmul(ps[:, 1, 0:TOP_K], ones[0:1, 0:128], rt[0:1, 22, 0:TOP_K], start=True,
                             stop=True).then_inc(tw_pe, 1)

            def hidden(b, par):
                for f in range(TOP_K * NF):
                    if f >= 4 or older(b, 1):
                        pe.wait_ge(gelu_done.sem, b * (TOP_K * NF) + f - 3)
                    for k in range(KD):
                        last = nc.tensor.matmul(ps[:, f % 4, 0:BT], w1s[:, f // NF, k, (f % NF) * 128:(f % NF + 1) * 128],
                                                hT[:, k, b, :], start=(k == 0), stop=(k == KD - 1))
                    last.then_inc(f_done.sem, 1)

            def result(b, par):
                for t in range(TB):
                    if older(b, 2):
                        pe.wait_ge(z.sem, z.count(b - 2))
                    for f in range(TOP_K * NF):
                        if t == 0:
                            pe.wait_ge(gelu_done.sem, gelu_done.count(b, f + 1))
                        last = nc.tensor.matmul(ps[0:TP, 4 + 2 * par + t, 0:D], ge[:, par, f, t * TP:(t + 1) * TP],
                                                w2s[:, f // NF, f % NF, :], start=(f == 0), stop=(f == TOP_K * NF - 1))
                    last.then_inc(y_done.sem, 1)

            pe.wait_ge(experts_in, 16 * (3 + 4 * TOP_K))
            pe.wait_ge(w_dve, 5)
            pipeline(pe, NB, [(0, hidden), (1, result)])

        @block.vector
        def _(dve):
            nc.vector.memset(pw[:, :, :].rearrange("p c n -> p (c n)"), 0.0).then_inc(prep, 1)
            nc.vector.memset(junk[:], 0.0).then_inc(prep, 1)

            per = NT // LOADS
            for i in range(LOADS):
                dve.wait_ge(x_in[i], 16)
                with dve.Fori(i * per, (i + 1) * per) as j:
                    nc.vector.bn_stats(st[0:TP, j, :], X[0:TP, j, :]).then_inc(sums_done, 1)
            dve.wait_ge(sums_done, NT)

            n = [0]

            def row(ins):
                n[0] += 1
                ins.then_inc(row_dve, 1)
                dve.wait_ge(row_dve, n[0])

            r = [rows[0:TP, i, :] for i in range(12)]
            s = [st[0:TP, :, i] for i in range(6)]
            row(nc.vector.tensor_tensor(r[0], s[1], s[4], ALU.add))
            row(nc.vector.tensor_scalar(r[0], r[0], 0.5, None, ALU.mult))
            row(nc.vector.tensor_tensor(r[1], s[1], s[4], ALU.subtract))
            row(nc.vector.tensor_tensor(r[1], r[1], r[1], ALU.mult))
            row(nc.vector.tensor_tensor(r[2], s[2], s[5], ALU.add))
            row(nc.vector.tensor_scalar(r[2], r[2], 1.0 / D, None, ALU.mult))
            row(nc.vector.scalar_tensor_tensor(out=r[3], in0=r[1], scalar=0.25, in1=r[2], op0=ALU.mult, op1=ALU.add))
            row(nc.vector.tensor_scalar(r[4], r[3], LN_EPS, None, ALU.add))
            assert n[0] == ROW_DVE1
            dve.wait_ge(row_pool, 1)
            row(nc.vector.tensor_tensor(r[6], r[3], r[5], ALU.mult))
            row(nc.vector.tensor_tensor(r[6], r[6], r[5], ALU.mult))
            assert n[0] == ROW_DVE2
            dve.wait_ge(row_pool, 2)
            row(nc.vector.tensor_scalar(r[7], r[7], math.sqrt(D), MIN_NORM, ALU.mult, ALU.max))
            row(nc.vector.tensor_scalar(r[8], r[7], MAXNORM, None, ALU.min))
            row(nc.vector.tensor_scalar(r[9], r[8], -1.0, 1.0, ALU.mult, ALU.add))
            row(nc.vector.reciprocal(r[9], r[9]))
            row(nc.vector.scalar_tensor_tensor(out=r[6], in0=r[8], scalar=1.0, in1=r[9], op0=ALU.add, op1=ALU.mult))
            assert n[0] == ROW_DVE3
            dve.wait_ge(row_ln, 1)
            row(nc.vector.reciprocal(r[7], r[7]))
            row(nc.vector.scalar_tensor_tensor(out=r[8], in0=r[8], scalar=0.5, in1=r[7], op0=ALU.mult, op1=ALU.mult))
            row(nc.vector.tensor_scalar(r[8], r[8], A_MAX / math.sqrt(D) * 0.9, None, ALU.max))
            row(nc.vector.reciprocal(r[10], r[8]))
            assert n[0] == ROW_DVE4
            row(nc.vector.tensor_tensor(r[11], r[8], r[5], ALU.mult))

            dve.wait_ge(w_in, 16 * W_IN)
            for side in range(2):
                for k in range(KD):
                    nc.vector.tensor_tensor(attp[:, side, k], wg[:, k, 0:D], attb[:, side], ALU.mult).then_inc(prep, 1)
            dve.wait_ge(prep, 2 + 2 * KD)
            for side in range(2):
                for k in range(KD):
                    last = nc.vector.tensor_reduce(
                        wg[:, k, D + side * HEADS:D + (side + 1) * HEADS],
                        attp[:, side, k].rearrange("p (h d) -> p h d", h=HEADS), AX.X, ALU.add)
            for c in range(NC):
                last = nc.vector.tensor_scalar(pw[:, c, :], pw[:, c, :], dwc[:, c:c + 1], None, ALU.mult)
            last.then_inc(prep, 1)
            dve.wait_ge(const, 7)

            def make_h(b, par):
                if older(b, 2):
                    dve.wait_ge(gram_done.sem, gram_done.count(b - 2))
                for t in range(TB):
                    j = b * TB + t
                    nc.vector.tensor_scalar(hb[0:TP, par, t, 0:D], X[0:TP, j, :], rows[0:TP, 0, bass.ds(j, 1)],
                                            rows[0:TP, 11, bass.ds(j, 1)], ALU.subtract,
                                            ALU.mult).then_inc(h_made.sem, 1)

            def keep_h(b, par):
                dve.wait_ge(h_out.sem, h_out.count(b))
                nc.vector.tensor_scalar(hT[:, :, b, :], hTs[:, par], 1.0, None, ALU.mult).then_inc(h_kept.sem, 1)
                for t in range(TB):
                    j = b * TB + t
                    dve.wait_ge(xt_made.sem, xt_made.count(b, t + 1))
                    if t == 0 and older(b, 2):
                        dve.wait_ge(xt_out[par], turns(b, par, 32))
                    nc.vector.tensor_scalar(xts[0:TP, par, t, :], ps[0:TP, 4 + t, 0:XT],
                                            rows[0:TP, 10, bass.ds(j, 1)], None, ALU.mult).then_inc(xt_ready.sem, 1)

            pipeline(dve, NB, [(0, make_h), (1, keep_h)])

            m = [0]

            def bn(ins, wait=True):
                m[0] += 1
                ins.then_inc(bn_dve, 1)
                if wait:
                    dve.wait_ge(bn_dve, m[0])

            dve.wait_ge(gram_done.sem, gram_done.count(NB - 1))
            bn(nc.vector.tensor_copy(gram[:, 0, :], ps[:, 2, 0:D + 1]), False)
            bn(nc.vector.tensor_copy(gram[:, 1, 128:D + 1], ps[:, 3, 0:D + 1 - 128]), False)
            dve.wait_ge(bn_pe, 1)
            bn(nc.vector.tensor_copy(gram[:, 1, 0:128], ps[:, 6, 0:128]), False)
            dve.wait_ge(bn_pe, 2)
            for k in range(KD):
                for i in range(2):
                    cs = slice(i * (CQ // 2), (i + 1) * (CQ // 2))
                    bn(nc.vector.tensor_tensor(wgw[:, k, cs], ps[:, 2 * k + i, 0:CQ // 2], wq[:, k, cs], ALU.mult), False)
            dve.wait_ge(bn_pe, 3)
            v = [bst[:, i, :] for i in range(8)]
            bn(nc.vector.tensor_scalar(v[0], ps[:, 7, NC:2 * NC], 1.0 / N, None, ALU.mult), False)
            bn(nc.vector.tensor_scalar(v[1], ps[:, 7, 0:NC], 1.0 / N, None, ALU.mult))
            assert m[0] == BN_READ
            bn(nc.vector.tensor_tensor(v[2], v[0], v[0], ALU.mult))
            bn(nc.vector.tensor_tensor(v[3], v[1], v[2], ALU.subtract))
            bn(nc.vector.tensor_scalar(v[4], v[3], 0.0, LN_EPS, ALU.max, ALU.add), False)
            assert m[0] == BN_VAR
            dve.wait_ge(bn_pool, 1)
            bn(nc.vector.tensor_tensor(bn_s[:], bng[:], v[5], ALU.mult))
            bn(nc.vector.tensor_tensor(v[6], v[0], bn_s[:], ALU.mult))
            bn(nc.vector.tensor_tensor(bn_o[:], bnb[:], v[6], ALU.subtract), False)
            assert m[0] == BN_DONE

            def keep_cat(b, par, t):
                dve.wait_ge(cat_done.sem, cat_done.count(b, t + 1))
                if older(b, 2):
                    dve.wait_ge(att.sem, att.count(b - 2, 6 * (t + 1)))
                    dve.wait_ge(cat_sq.sem, cat_sq.count(b - 2, t + 1))
                nc.vector.tensor_copy(cat[0:TP, par, t, :], ps[0:TP, 2:5, :].rearrange("p a n -> p (a n)")
                                      ).then_inc(cat_out.sem, 1)

            def attention(b, par, t):
                k0, a = 6 * t, att
                c = cat[0:TP, par, t].rearrange("p (g c) -> p g c", c=3 * GROUP)
                if t == 1 or older(b, 1):
                    dve.wait_ge(a.sem, b * a.per + k0)
                nc.vector.tensor_reduce(ksum[0:TP, 0:GC // 2], c[:, 0:GC // 2, GROUP:2 * GROUP], AX.X,
                                        ALU.add).then_inc(a.sem, 1)
                dve.wait_ge(kv_ready.sem, kv_ready.count(b, 2 * t + 2))
                nc.vector.tensor_reduce(ksum[0:TP, GC // 2:GC], krel[0:TP, t], AX.X, ALU.add).then_inc(a.sem, 1)
                nc.vector.reciprocal(rv[0:TP], veps[0:TP, t]).then_inc(a.sem, 1)
                dve.wait_ge(a.sem, a.count(b, k0 + 2))
                nc.vector.scalar_tensor_tensor(
                    out=qk[0:TP], in0=c[:, :, 0:GROUP], scalar=0.0,
                    in1=ksum[0:TP, :].rearrange("p (g a) -> p g a", a=1).broadcast_to([TP, GC, GROUP]),
                    op0=ALU.max, op1=ALU.mult).then_inc(a.sem, 1)
                dve.wait_ge(a.sem, a.count(b, k0 + 3))
                nc.vector.tensor_tensor(vr[0:TP], c[:, :, 2 * GROUP:], rv[0:TP], ALU.mult).then_inc(a.sem, 1)
                dve.wait_ge(a.sem, a.count(b, k0 + 5))
                if t == 0 and older(b, 2):
                    dve.wait_ge(o_turned.sem, o_turned.count(b - 2))
                    dve.wait_ge(att_sq.sem, att_sq.count(b - 2))
                nc.vector.tensor_tensor(ob[0:TP, par, t].rearrange("p (g c) -> p g c", c=GROUP), qk[0:TP], vr[0:TP],
                                        ALU.mult).then_inc(a.sem, 1)

            def make_u(b, par):
                dve.wait_ge(res_done.sem, res_done.count(b))
                dve.wait_ge(scale_e.sem, scale_e.count(b))
                if older(b, 2):
                    dve.wait_ge(u_sq.sem, u_sq.count(b - 2))
                for t in range(TB):
                    nc.vector.scalar_tensor_tensor(out=u[0:TP, par, t], in0=ps[0:TP, 6, t * D:(t + 1) * D],
                                                   scalar=se[0:TP, par, 5, t:t + 1], in1=brow[0:TP, :],
                                                   op0=ALU.mult, op1=ALU.add).then_inc(u_made.sem, 1)

            def edge_logits(b, par):
                e = edge
                dve.wait_ge(gathered[par], turns(b, par, 32 * TB, 32 * TB))
                if older(b, 1):
                    dve.wait_ge(e.sem, e.count(b - 1))
                nc.vector.tensor_tensor(at[0:TP, 0], asrc[0:TP, par], xg[0:TP, par, :, D + HEADS:XT],
                                        ALU.add).then_inc(e.sem, 1)
                dve.wait_ge(e.sem, e.count(b, 1))
                nc.vector.scalar_tensor_tensor(out=at[0:TP, 1], in0=at[0:TP, 0], scalar=0.01, in1=at[0:TP, 0],
                                               op0=ALU.mult, op1=ALU.max).then_inc(e.sem, 1)
                dve.wait_ge(e.sem, e.count(b, 2))
                nc.vector.tensor_reduce(atm[0:TP, 0], at[0:TP, 1], AX.X, ALU.max).then_inc(e.sem, 1)
                dve.wait_ge(e.sem, e.count(b, 3))
                nc.vector.tensor_tensor(at[0:TP, 3], at[0:TP, 1],
                                        atm[0:TP, 0].rearrange("p (t a) -> p t a", a=1).broadcast_to([TP, TB, HEADS]),
                                        ALU.subtract).then_inc(e.sem, 1)

            def edge_sum(b, par):
                e = edge
                dve.wait_ge(edge_exp.sem, edge_exp.count(b))
                nc.vector.tensor_reduce(atm[0:TP, 1], at[0:TP, 4], AX.X, ALU.add).then_inc(e.sem, 1)
                dve.wait_ge(e.sem, e.count(b, 5))
                nc.vector.reciprocal(atm[0:TP, 2], atm[0:TP, 1]).then_inc(e.sem, 1)
                dve.wait_ge(e.sem, e.count(b, 6))
                nc.vector.tensor_tensor(at[0:TP, 5], at[0:TP, 4],
                                        atm[0:TP, 2].rearrange("p (t a) -> p t a", a=1).broadcast_to([TP, TB, HEADS]),
                                        ALU.mult).then_inc(e.sem, 1)
                for t in range(TB):
                    dve.wait_ge(e.sem, e.count(b, 7 + 2 * t))
                    nc.vector.tensor_tensor(
                        gprod[0:TP].rearrange("p (h d) -> p h d", h=HEADS),
                        xg[0:TP, par, t, 0:D].rearrange("p (h d) -> p h d", h=HEADS),
                        at[0:TP, 5, t].rearrange("p (h a) -> p h a", a=1).broadcast_to([TP, HEADS, HD]),
                        ALU.mult).then_inc(e.sem, 1)
                    dve.wait_ge(e.sem, e.count(b, 8 + 2 * t))
                    if older(b, 2):
                        dve.wait_ge(x1.sem, x1.count(b - 2))
                    nc.vector.tensor_reduce(gt[0:TP, par, t], gprod[0:TP].rearrange("p (h d) -> p d h", h=HEADS),
                                            AX.X, ALU.add).then_inc(e.sem, 1)

            def make_x1(b, par):
                dve.wait_ge(scale_g.sem, scale_g.count(b))
                dve.wait_ge(edge.sem, edge.count(b))
                if older(b, 2):
                    dve.wait_ge(rstd_done.sem, rstd_done.count(b - 2))
                for t in range(TB):
                    j = b * TB + t
                    nc.vector.scalar_tensor_tensor(out=X[0:TP, j, :], in0=u[0:TP, par, t], scalar=sg[0:TP, par, 5, t:t + 1],
                                                   in1=X[0:TP, j, :], op0=ALU.mult, op1=ALU.add).then_inc(x1.sem, 1)
                    dve.wait_ge(x1.sem, x1.count(b, 4 * t + 1))
                    xh = X[0:TP, j, :].rearrange("p (h d) -> p h d", h=HEADS)
                    nc.vector.tensor_tensor(
                        xh, xh, gt[0:TP, par, t].rearrange("p (a d) -> p a d", a=1).broadcast_to([TP, HEADS, HD]),
                        ALU.add).then_inc(x1.sem, 1)
                    wait_apart(dve, x1, x1.count(b, 4 * t + 2), passed)
                    nc.vector.bn_stats(st2[0:TP, t], X[0:TP, j, :]).then_inc(x1.sem, 1)
                    wait_apart(dve, x1, x1.count(b, 4 * t + 3), passed)
                    nc.vector.bn_aggr(mv2[0:TP, par, t], st2[0:TP, t]).then_inc(x1.sem, 1)

            def make_xn(b, par):
                dve.wait_ge(rstd_done.sem, rstd_done.count(b))
                if older(b, 2):
                    dve.wait_ge(xn_turned.sem, xn_turned.count(b - 2))
                for t in range(TB):
                    nc.vector.tensor_scalar(xn[0:TP, par, t], X[0:TP, b * TB + t, :], mv2[0:TP, par, t, 0:1],
                                            r2[0:TP, par, 1, t:t + 1], ALU.subtract, ALU.mult).then_inc(xn_made.sem, 1)
                nc.vector.tensor_scalar(mean2[0:TP, bass.ds(b * TB, TB)], mv2[0:TP, par, :, 0], 1.0, None,
                                        ALU.mult).then_inc(xn_made.sem, 1)
                nc.vector.tensor_scalar(rstd2[0:TP, bass.ds(b * TB, TB)], r2[0:TP, par, 1], 1.0, None,
                                        ALU.mult).then_inc(xn_made.sem, 1)

            def keep_xn(b, par):
                dve.wait_ge(xn_turned.sem, xn_turned.count(b))
                nc.vector.tensor_scalar(hT[:, :, b, :], ps[:, 7, 0:KD * BT].rearrange("p (k n) -> p k n", k=KD), 1.0,
                                        None, ALU.mult).then_inc(xn_kept.sem, 1)
                dve.wait_ge(xn_kept.sem, xn_kept.count(b, 1))
                nc.vector.tensor_reduce(rsum[:, :, b], hT[:, :, b, :], AX.X, ALU.add).then_inc(xn_kept.sem, 1)

            dve.wait_ge(late_in, 16 * LATE)
            pipeline(dve, NB, [
                (6, keep_xn),
                (5, make_xn),
                (3, edge_logits),
                (1, lambda b, p: keep_cat(b, p, 0)),
                (2, lambda b, p: attention(b, p, 0)),
                (3, make_u),
                (3, edge_sum),
                (1, lambda b, p: keep_cat(b, p, 1)),
                (2, lambda b, p: attention(b, p, 1)),
                (4, make_x1),
            ])

            q = [0]

            def route(ins, wait=True):
                q[0] += 1
                ins.then_inc(rt_dve, 1)
                if wait:
                    dve.wait_ge(rt_dve, q[0])

            R = [rt[0:1, i, :] for i in range(24)]
            one = lambda i, k=0: rt[0:1, i, k:k + 1]
            dve.wait_ge(xn_kept.sem, xn_kept.count(NB - 1))
            route(nc.vector.tensor_reduce(rtot[:, :], rsum[:, :, :], AX.X, ALU.add))
            dve.wait_ge(rt_pe, 1)
            dve.wait_ge(experts_in, 48)
            route(nc.vector.scalar_tensor_tensor(out=R[0], in0=ps[0:1, 0, 0:EX], scalar=1.0 / N, in1=rt_b[:],
                                                 op0=ALU.mult, op1=ALU.add))

            def softmax(src, base, act_count):
                route(nc.vector.tensor_reduce(one(base + 2), R[src], AX.X, ALU.max))
                route(nc.vector.tensor_scalar(R[base], R[src], one(base + 2), None, ALU.subtract))
                at_exp = q[0]
                dve.wait_ge(rt_act, act_count)
                route(nc.vector.tensor_reduce(one(base + 2, 1), R[base + 1], AX.X, ALU.add))
                route(nc.vector.reciprocal(one(base + 2, 2), one(base + 2, 1)))
                route(nc.vector.tensor_scalar(R[base + 3], R[base + 1], one(base + 2, 2), None, ALU.mult))
                return at_exp

            assert softmax(0, 1, 1) == RT_E1
            route(nc.vector.tensor_scalar(R[4], R[4], CAP, None, ALU.min))
            assert softmax(4, 5, 2) == RT_E2
            route(nc.vector.tensor_scalar(R[9], iota[:], 100.0, None, ALU.add))
            for i in range(TOP_K):
                route(nc.vector.tensor_reduce(one(10, i), R[8], AX.X, ALU.max))
                route(nc.vector.tensor_scalar(R[11], R[8], one(10, i), None, ALU.is_equal))
                route(nc.vector.scalar_tensor_tensor(out=R[12], in0=R[11], scalar=-100.0, in1=R[9],
                                                     op0=ALU.mult, op1=ALU.add))
                route(nc.vector.tensor_reduce(one(13, i), R[12], AX.X, ALU.min))
                route(nc.vector.tensor_scalar(R[14], iota[:], one(13, i), None, ALU.is_equal))
                route(nc.vector.scalar_tensor_tensor(out=R[8], in0=R[14], scalar=-10.0, in1=R[8],
                                                     op0=ALU.mult, op1=ALU.add))
            route(nc.vector.tensor_copy(chosen[:], rt[0:1, 13, 0:TOP_K]))
            assert q[0] == RT_CHOSEN
            route(nc.vector.tensor_tensor(one(18), one(10, 1), one(10, 0), ALU.subtract))
            assert q[0] == RT_E3
            dve.wait_ge(rt_act, 3)
            route(nc.vector.tensor_scalar(one(20), one(19), 1.0, None, ALU.add))
            route(nc.vector.reciprocal(one(22, 0), one(20)))
            route(nc.vector.tensor_tensor(one(22, 1), one(19), one(22, 0), ALU.mult))
            assert q[0] == RT_TW
            dve.wait_ge(tw_pe, 1)
            nc.vector.tensor_copy(tw[:], ps[:, 1, 0:TOP_K]).then_inc(w_dve, 1)
            dve.wait_ge(w_dve, 1)
            dve.wait_ge(experts_in, 16 * (3 + 4 * TOP_K))
            for i in range(TOP_K):
                wi = w2s[:, i].rearrange("p f d -> p (f d)")
                nc.vector.tensor_scalar(wi, wi, tw[:, i:i + 1], None, ALU.mult).then_inc(w_dve, 1)
            nc.vector.tensor_scalar(b2w[0:TP], b2s[0:TP, 0], tw[0:TP, 0:1], None, ALU.mult).then_inc(w_dve, 1)
            dve.wait_ge(w_dve, 4)
            nc.vector.scalar_tensor_tensor(out=b2w[0:TP], in0=b2s[0:TP, 1], scalar=tw[0:TP, 1:2], in1=b2w[0:TP],
                                           op0=ALU.mult, op1=ALU.add).then_inc(w_dve, 1)
            dve.wait_ge(w_dve, 5)

            def make_z(b, par):
                if older(b, 2):
                    dve.wait_ge(y_ready.sem, y_ready.count(b - 2))
                for t in range(TB):
                    j = b * TB + t
                    nc.vector.tensor_scalar(za[0:TP, par, t], X[0:TP, j, :], mean2[0:TP, bass.ds(j, 1)],
                                            rstd2[0:TP, bass.ds(j, 1)], ALU.subtract, ALU.mult).then_inc(z.sem, 1)
                    dve.wait_ge(z.sem, z.count(b, 5 * t + 1))
                    nc.vector.tensor_tensor(za[0:TP, par, t], za[0:TP, par, t], b2w[0:TP], ALU.add).then_inc(z.sem, 1)
                    dve.wait_ge(z.sem, z.count(b, 5 * t + 2))
                    dve.wait_ge(y_done.sem, y_done.count(b, t + 1))
                    nc.vector.tensor_tensor(zz[0:TP, par, t], ps[0:TP, 4 + 2 * par + t, 0:D], za[0:TP, par, t],
                                            ALU.add).then_inc(z.sem, 1)
                    wait_apart(dve, z, z.count(b, 5 * t + 3), passed)
                    nc.vector.bn_stats(zst[0:TP, t], zz[0:TP, par, t]).then_inc(z.sem, 1)
                    wait_apart(dve, z, z.count(b, 5 * t + 4), passed)
                    nc.vector.bn_aggr(zmv[0:TP, par, t], zst[0:TP, t]).then_inc(z.sem, 1)

            def norm_z(b, par):
                dve.wait_ge(z_rstd.sem, z_rstd.count(b))
                for t in range(TB):
                    nc.vector.tensor_scalar(zz[0:TP, par, t], zz[0:TP, par, t], zmv[0:TP, par, t, 0:1],
                                            zr[0:TP, par, 1, t:t + 1], ALU.subtract, ALU.mult).then_inc(z_norm.sem, 1)

            def make_y(b, par):
                if older(b, 2):
                    dve.wait_ge(y_out[par], turns(b, par, 16))
                for t in range(TB):
                    dve.wait_ge(z_gam.sem, z_gam.count(b, 2 * t + 2))
                    nc.vector.tensor_tensor(yo[0:TP, par, t, :], zz[0:TP, par, t], X[0:TP, b * TB + t, :],
                                            ALU.add).then_inc(y_ready.sem, 1)

            pipeline(dve, NB, [(1, make_z), (2, norm_z), (2, make_y)])


def kernel(x, src, dst, L0_gnn_weight, L0_gnn_attn_l, L0_gnn_attn_r, L0_mix_w_qkv, L0_mix_bn_gamma, L0_mix_bn_beta,
           L0_mix_w_dw, L0_mix_w_pw, L0_mix_w_res, L0_mix_b_res, L0_ffn_Wr, L0_ffn_br, L0_ffn_W1, L0_ffn_b1,
           L0_ffn_W2, L0_ffn_b2, L0_ffn_gamma, L0_ffn_beta):
    import numpy as np
    import concourse.bacc as bacc
    from concourse.bass_utils import run_bass_kernel_spmd

    n = x.shape[0]
    tiles = lambda a: np.asarray(a)[:n].reshape(-1, TP, TB).transpose(1, 0, 2).reshape(TP, -1)
    columns = lambda a: np.asarray(a).reshape(-1, 128).T
    pw = np.asarray(L0_mix_w_pw)[:, :, 0]
    ins = {
        "x": x,
        "idx_dst": tiles(dst),
        "idx_src": tiles(src),
        "w_gnn": L0_gnn_weight,
        "attn_l": L0_gnn_attn_l,
        "attn_r": L0_gnn_attn_r,
        "w_qkv": np.asarray(L0_mix_w_qkv)[:, :, 2].T,
        "bn_gamma": columns(L0_mix_bn_gamma),
        "bn_beta": columns(L0_mix_bn_beta),
        "w_dw": columns(np.asarray(L0_mix_w_dw)[:, 0, 2]),
        "w_pw": pw.reshape(-1, GROUP, GROUP).transpose(0, 2, 1),
        "w_res": np.asarray(L0_mix_w_res)[:, :, 0].T,
        "b_res": L0_mix_b_res,
        "w_router": L0_ffn_Wr,
        "b_router": L0_ffn_br,
        "w1": L0_ffn_W1,
        "b1": L0_ffn_b1,
        "w2": L0_ffn_W2,
        "b2": L0_ffn_b2,
        "gamma": L0_ffn_gamma,
        "beta": L0_ffn_beta,
    }
    nc = bacc.Bacc("TRN2", target_bir_lowering=False, num_devices=1)
    arrays, args = {}, []
    for name, a in ins.items():
        a = np.ascontiguousarray(a)
        arrays[f"in_{name}"] = a
        args.append(nc.dram_tensor(f"in_{name}", a.shape, mybir.dt.from_np(a.dtype), kind="ExternalInput").ap())
    out = nc.dram_tensor("out", x.shape, F32, kind="ExternalOutput").ap()
    gps_layer(nc, *args, out)
    r = run_bass_kernel_spmd(nc, [arrays], core_ids=[0])
    return r.results[0]["out"]
```
